# Optimizing a Trainium2 kernel written in Bass

```python
import numpy as np
import jax
import jax.numpy as jnp

def _softmax(x, axis=-1):
    return jax.nn.softmax(x, axis=axis)

def _gelu(x):
    return jax.nn.gelu(x, approximate=True)

def _silu(x):
    return jax.nn.silu(x)

def _sigmoid(x):
    return jax.nn.sigmoid(x)

def _layernorm(x, axis=-1, eps=1e-05):
    m = jnp.mean(x, axis=axis, keepdims=True)
    v = jnp.var(x, axis=axis, keepdims=True)
    return (x - m) / jnp.sqrt(v + eps)

def _scatter_add(tgt, idx, src, axis=0):
    return tgt.at[idx].add(src)

def _segment_sum(src, seg, n):
    return jax.ops.segment_sum(src, seg, n)
kernel_name = 'mk_rec_standalone_d1_rec_r8_c379e7'

def setup_inputs(seed: int=0):
    np.random.seed(seed)
    _w = jnp.asarray

    def _rec_inputs():
        import jax
        import jax.numpy as jnp
        _rk = jax.random.key(seed)
        r_x = -0.000292821 + 1.00034 * jax.random.normal(jax.random.fold_in(_rk, 1), (512, 64, 32), jnp.float32)
        return r_x
    r_x = _rec_inputs()

    def _L0_rec_setup():
        import jax, jax.numpy as jnp
        import numpy as np
        B, F, E = (256, 64, 32)
        H1, H2 = (64, 64)

        def _cin_layer(x0, hidden, W, b, n_fields, h_prev):
            Wr = W.reshape(W.shape[0], n_fields, h_prev)
            z = jnp.einsum('ofh,bef,beh->boe', Wr, x0, hidden) + b[:, None]
            return jax.nn.relu(z)
        key = jax.random.key(seed)
        k_x, k_w1, k_b1, k_w2, k_b2 = jax.random.split(key, 5)
        x = jax.random.normal(k_x, (B, F, E), dtype=jnp.float32)
        lim1 = float(np.sqrt(6.0 / (F * F + 2 * H1)))
        W1 = jax.random.uniform(k_w1, (2 * H1, F * F), jnp.float32, -lim1, lim1)
        b1 = jnp.zeros((2 * H1,), jnp.float32)
        lim2 = float(np.sqrt(6.0 / (F * H1 + H2)))
        W2 = jax.random.uniform(k_w2, (H2, F * H1), jnp.float32, -lim2, lim2)
        b2 = jnp.zeros((H2,), jnp.float32)
        return {'x': x, 'W1': W1, 'b1': b1, 'W2': W2, 'b2': b2}
    _L0_rec_all = _L0_rec_setup()
    _L0_rec_in = {k: v for k, v in _L0_rec_all.items() if k in ('W1', 'b1', 'W2', 'b2')}
    del _L0_rec_all
    return {'r_x': r_x, 'L0_rec_W1': _L0_rec_in['W1'], 'L0_rec_b1': _L0_rec_in['b1'], 'L0_rec_W2': _L0_rec_in['W2'], 'L0_rec_b2': _L0_rec_in['b2']}

def reference(r_x, L0_rec_W1, L0_rec_b1, L0_rec_W2, L0_rec_b2):
    import jax
    import jax.numpy as jnp

    def _L0_rec_ref(x, W1, b1, W2, b2):
        import jax, jax.numpy as jnp
        import numpy as np
        B, F, E = (256, 64, 32)
        H1, H2 = (64, 64)

        def _cin_layer(x0, hidden, W, b, n_fields, h_prev):
            Wr = W.reshape(W.shape[0], n_fields, h_prev)
            z = jnp.einsum('ofh,bef,beh->boe', Wr, x0, hidden) + b[:, None]
            return jax.nn.relu(z)
        x0 = jnp.transpose(x, (0, 2, 1))
        z1 = _cin_layer(x0, x0, W1, b1, F, F)
        direct1, nxt = (z1[:, :H1, :], z1[:, H1:, :])
        hidden1 = jnp.transpose(nxt, (0, 2, 1))
        z2 = _cin_layer(x0, hidden1, W2, b2, F, H1)
        out = jnp.concatenate([direct1, z2], axis=1)
        return jnp.sum(out, axis=-1)
    y = _L0_rec_ref(r_x, L0_rec_W1, L0_rec_b1, L0_rec_W2, L0_rec_b2)
    return y

_drawn_inputs = setup_inputs


def setup_inputs(seed=0):
    import zlib

    import numpy as np

    out = dict(_drawn_inputs(seed))
    spreads = {'L0_rec_b1': (0.0, 0.1), 'L0_rec_b2': (0.0, 0.1)}
    factors = {}
    for name, (base, spread) in spreads.items():
        noise = np.random.default_rng([zlib.crc32(name.encode()), seed]).standard_normal(out[name].shape)
        drawn = base * np.exp(spread * noise) if base else spread * noise
        out[name] = jnp.asarray(drawn.astype(out[name].dtype))
    for name, factor in factors.items():
        out[name] = (out[name] * factor).astype(out[name].dtype)
    return out
```

```python
import concourse.bass as bass
from concourse import mybir
from contextlib import ExitStack

F = 64
O1, O2 = 128, 64
E = 32
W = 512
BT = W // E
NT = 8
NC1, NC2 = 2, 4
G = 4
NA = NC1 * NT // G
HG = NT // G
NB = (NC2 - 1) * HG
NP = HG
RING = 5
SLOTS = 3
LEAD = NA
STEP = NA + NB
AFTER_B = 4


def build(nc, turned, dup, w1, w1_swapped, w2, partner, b1, b2, out_direct, out_second):
    f32 = mybir.dt.float32
    ALU = mybir.AluOpType
    ACT = mybir.ActivationFunctionType
    AX = mybir.AxisListType
    tiles = turned.shape[0]
    LOOPS = (tiles - 2) // SLOTS
    assert 1 + SLOTS * LOOPS == tiles - 1 and STEP % RING == 0

    ctx = ExitStack()
    with ctx:
        def sb(name, shape):
            return ctx.enter_context(nc.sbuf_tensor(name, shape, f32))

        def pb(name, shape):
            return ctx.enter_context(nc.psum_tensor(name, shape, f32))

        def sem(name):
            return ctx.enter_context(nc.semaphore(name))

        R = sb("R", [128, SLOTS, NT, W])
        V = sb("V", [128, SLOTS, NC1, W])
        far = sb("far", [32, SLOTS, 2, W])
        w1_sb = sb("w1_sb", [128, NC1 * NT + 1, O1])
        w1_sw = sb("w1_sw", [128, NC1 * NT + 1, O1])
        w2_sb = sb("w2_sb", [128, NC2 * NT, O2])
        partner_sb = sb("partner_sb", [128, 1])
        b1_sb = sb("b1_sb", [O1, 1])
        b2_sb = sb("b2_sb", [2 * O2, 1])
        z = sb("z", [128, RING, G, W])
        zp = sb("zp", [128, NP, G, W])
        zs = sb("zs", [32, SLOTS, W])
        hid = sb("hid", [128, W])
        Hd = sb("Hd", [128, SLOTS, W])
        direct = sb("direct", [64, W])
        second = sb("second", [128, W // 2])
        sum_direct = sb("sum_direct", [64, tiles, BT])
        sum_second = sb("sum_second", [128, tiles, BT // 2])
        Vp = pb("Vp", [128, NC1, W])
        Hp = pb("Hp", [128, NC2 - 1, W])
        acc1 = pb("acc1", [O1, W])
        acc2 = pb("acc2", [2 * O2, W])

        w1_loaded = sem("w1_loaded")
        w2_loaded = sem("w2_loaded")
        w1_ready = sem("w1_ready")
        r_loaded = [sem(f"r_loaded{s}") for s in range(SLOTS)]
        v_loaded = [sem(f"v_loaded{s}") for s in range(SLOTS)]
        v_ready = sem("v_ready")
        h_ready = sem("h_ready")
        hid_ready = sem("hid_ready")
        hd_loaded = sem("hd_loaded")
        direct_ready = sem("direct_ready")
        second_ready = sem("second_ready")
        direct_summed = sem("direct_summed")
        second_summed = sem("second_summed")
        z_made = sem("z_made")
        z_used = sem("z_used")
        zp_made = sem("zp_made")
        zp_used = sem("zp_used")
        zs_made = sem("zs_made")
        stored = sem("stored")

        block = ctx.enter_context(nc.Block())

        def tile(n, k):
            return SLOTS * n + k

        def times(n, k, count, more=0):
            return n * (SLOTS * count) + (k * count + more)

        def is_first(n, k):
            return isinstance(n, int) and (n, k) == (0, 0)

        def rounds(n, k):
            return n + k // SLOTS + 1

        def ahead(n, k):
            return 0 if isinstance(n, int) and tile(n, k) == tiles - 1 else NA

        def a_group(n, k, a):
            return times(n, k - 1, STEP, LEAD + a)

        def b_group(n, k, b):
            return times(n, k, STEP, LEAD + ahead(n, k) + b)

        def steps(engine, step):
            step(0, 0)
            with engine.Fori(0, LOOPS) as n:
                for k in range(1, 1 + SLOTS):
                    step(n, k)

        @block.sync
        def _(sp):
            def addresses(n, k):
                at = (times(n, k, 160 * W), times(n, k, 160 * W, 32 * W), times(n, k, 156 * W))
                return at if isinstance(n, int) else tuple(sp.snap(v) for v in at)

            def load(n, k, at):
                s = k % SLOTS
                sp.dma_start(V[:, s, :, :],
                             bass.AP(tensor=dup.tensor, offset=at[0],
                                     ap=[[W, 128], [32 * W, NC1], [1, W]])).then_inc(v_loaded[s], 16)
                sp.dma_start(far[:, s, :, :],
                             bass.AP(tensor=dup.tensor, offset=at[1],
                                     ap=[[2 * W, 32], [64 * W, 2], [1, W]])).then_inc(v_loaded[s], 16)
                sp.dma_start(R[:, s, :, :],
                             bass.AP(tensor=turned.tensor, offset=at[2],
                                     ap=[[W, 128], [4 * W, NT], [1, W]])).then_inc(r_loaded[s], 16)

            def reload(n, k):
                at = addresses(n, k)
                sp.wait_ge(z_used, b_group(n, k - SLOTS, NB))
                load(n, k, at)

            sp.dma_start(w1_sb[:], w1).then_inc(w1_loaded, 16)
            sp.dma_start(w1_sw[:], w1_swapped).then_inc(w1_loaded, 16)
            sp.dma_start(b1_sb[:], b1).then_inc(w1_loaded, 16)
            sp.dma_start(partner_sb[:], partner).then_inc(w1_loaded, 16)
            load(0, 0, addresses(0, 0))
            load(0, 1, addresses(0, 1))
            sp.dma_start(w2_sb[:], w2).then_inc(w2_loaded, 16)
            sp.dma_start(b2_sb[:], b2).then_inc(w2_loaded, 16)
            load(0, 2, addresses(0, 2))
            loads = (tiles - SLOTS) // SLOTS
            with sp.Fori(1, 1 + loads) as n:
                for k in range(SLOTS):
                    reload(n, k)
            for k in range((tiles - SLOTS) % SLOTS):
                reload(1 + loads, k)
            sp.wait_ge(direct_summed, tiles)
            sp.dma_start(out_direct, sum_direct[:]).then_inc(stored, 16)
            sp.wait_ge(second_summed, tiles)
            sp.dma_start(out_second, sum_second[:]).then_inc(stored, 16)
            sp.wait_ge(stored, 32)

        @block.scalar
        def _(act):
            def copy_v(n, k):
                act.wait_ge(v_loaded[k % SLOTS], 32 * rounds(n, k))
                nc.scalar.activation(Vp[:], V[:, k % SLOTS, :, :], ACT.Copy).then_inc(v_ready, 1)

            def turn_h(n, k):
                act.wait_ge(hd_loaded, times(n, k + 1, 32))
                s = k % SLOTS
                for c in range(1, NC2):
                    size = 64 if c == 2 else 32
                    for q in range(0, 128, size):
                        to = (q + 32 * c) % 128
                        last = nc.scalar.activation(Hp[to:to + size, c - 1, :], Hd[q:q + size, s, :], ACT.Copy)
                last.then_inc(h_ready, 1)

            def take_z1(n, k, done):
                act.wait_ge(z_used, done)
                j = tile(n, k)
                act.wait_ge(hd_loaded, times(n, k, 32))
                nc.scalar.activation(hid[64:128, :], acc1[64:128, :], ACT.Relu,
                                     bias=b1_sb[64:128, :]).then_inc(hid_ready, 1)
                act.wait_ge(direct_summed, j)
                nc.scalar.activation(direct[:], acc1[0:64, :], ACT.Relu,
                                     bias=b1_sb[0:64, :]).then_inc(direct_ready, 1)
                act.wait_ge(hid_ready, j + 1)
                for r in range(2):
                    act.dma_start(Hd[r::2, k % SLOTS, :], hid[64:128, :]).then_inc(hd_loaded, 16)

            def take_z2(n, k):
                act.wait_ge(z_used, b_group(n, k, NB))
                nc.scalar.activation(second[:], acc2[:, 0:W // 2], ACT.Relu,
                                     bias=b2_sb[:]).then_inc(second_ready, 1)

            def step(n, k):
                act.wait_ge(z_made, LEAD if is_first(n, k) else a_group(n, k, NA))
                copy_v(n, k + 1)
                if not is_first(n, k):
                    act.wait_ge(z_made, b_group(n, k - 1, NB))
                turn_h(n, k)
                if not is_first(n, k):
                    take_z2(n, k - 1)
                take_z1(n, k + 1, a_group(n, k + 1, NA))

            act.wait_ge(w1_loaded, 64)
            copy_v(0, 0)
            take_z1(0, 0, LEAD)
            act.wait_ge(w2_loaded, 32)
            steps(act, step)
            n, k = LOOPS, 1
            act.wait_ge(z_made, b_group(n, k - 1, NB))
            turn_h(n, k)
            take_z2(n, k - 1)
            act.wait_ge(second_summed, tile(n, k))
            take_z2(n, k)

        @block.vector
        def _(dve):
            def products(group, ring, other, n, k, c, half):
                if not isinstance(group, int) or group >= RING:
                    dve.wait_ge(z_used, group - RING + 1)
                s = k % SLOTS
                nc.vector.tensor_tensor(
                    z[:, ring % RING, :, :], other.unsqueeze(1).to_broadcast([128, G, W]),
                    R[:, s, half * G:(half + 1) * G, :], ALU.mult).then_inc(z_made, 1)

            def layer1(n, k, first, ring):
                dve.wait_ge(r_loaded[k % SLOTS], 16 * rounds(n, k))
                dve.wait_ge(v_ready, tile(n, k) + 1)
                for a in range(NA):
                    products(first + a, ring + a, Vp[:, NC1 - 1 - a // HG, :], n, k, a // HG, a % HG)

            def sum_z1(n, k):
                j = tile(n, k)
                dve.wait_ge(direct_ready, j + 1)
                nc.vector.tensor_reduce(sum_direct[:, bass.ds(j, 1), :].rearrange("p o b -> p (o b)"),
                                        direct[:].rearrange("p (b e) -> p b e", e=E),
                                        AX.X, ALU.add).then_inc(direct_summed, 1)

            def sum_z2(n, k):
                j = tile(n, k)
                dve.wait_ge(second_ready, j + 1)
                nc.vector.tensor_reduce(sum_second[:, bass.ds(j, 1), :].rearrange("p o b -> p (o b)"),
                                        second[:].rearrange("p (b e) -> p b e", e=E),
                                        AX.X, ALU.add).then_inc(second_summed, 1)

            def layer2(n, k):
                dve.wait_ge(h_ready, tile(n, k) + 1)
                for b in range(NB):
                    if b == AFTER_B:
                        sum_z1(n, k)
                        if not is_first(n, k):
                            sum_z2(n, k - 1)
                    products(b_group(n, k, b), LEAD + ahead(n, k) + b, Hp[:, b // HG, :], n, k, 1 + b // HG, b % HG)

            def step(n, k):
                layer1(n, k + 1, a_group(n, k + 1, 0), LEAD)
                layer2(n, k)

            dve.wait_ge(w1_loaded, 64)
            nc.vector.tensor_tensor(w1_sb[:, 1:, :], w1_sb[:, 1:, :], w1_sw[:, 1:, :], ALU.add).then_inc(w1_ready, 1)
            nc.vector.scalar_tensor_tensor(out=w1_sb[:, 0, :], in0=w1_sw[:, 0, :], scalar=partner_sb[:, 0:1],
                                           in1=w1_sb[:, 0, :], op0=ALU.mult, op1=ALU.add).then_inc(w1_ready, 1)
            layer1(0, 0, 0, 0)
            steps(dve, step)
            n, k = LOOPS, 1
            layer2(n, k)
            sum_z2(n, k)

        @block.gpsimd
        def _(pool):
            def far_products(n, k):
                pool.wait_ge(v_loaded[k % SLOTS], 32 * rounds(n, k))
                s = k % SLOTS
                nc.gpsimd.tensor_tensor(zs[:, s, :], far[:, s, 0, :], far[:, s, 1, :],
                                        ALU.mult).then_inc(zs_made, 1)

            def layer2(n, k):
                s = k % SLOTS
                pool.wait_ge(r_loaded[s], 16 * rounds(n, k))
                pool.wait_ge(hd_loaded, times(n, k + 1, 32))
                for g in range(NP):
                    if not is_first(n, k):
                        pool.wait_ge(zp_used, times(n, k - 1, NP, g + 1))
                    nc.gpsimd.tensor_tensor(
                        zp[:, g, :, :], Hd[:, s, :].unsqueeze(1).to_broadcast([128, G, W]),
                        R[:, s, g * G:(g + 1) * G, :], ALU.mult).then_inc(zp_made, 1)

            def step(n, k):
                far_products(n, k + 1)
                layer2(n, k)

            far_products(0, 0)
            steps(pool, step)
            layer2(LOOPS, 1)

        @block.tensor
        def _(pe):
            def layer1(n, k, first, ring):
                j = tile(n, k)
                pe.wait_ge(zs_made, j + 1)
                if not is_first(n, k):
                    pe.wait_ge(direct_ready, j)
                nc.tensor.matmul(acc1[:], w1_sb[0:32, NC1 * NT, :], zs[:, k % SLOTS, :],
                                 start=True, stop=False)
                for a in range(NA):
                    pe.wait_ge(z_made, first + a + 1)
                    for g in range(G):
                        last = nc.tensor.matmul(acc1[:], w1_sb[:, a * G + g, :], z[:, (ring + a) % RING, g, :],
                                                start=False, stop=(a == NA - 1 and g == G - 1))
                    last.then_inc(z_used, 1)

            def contract2(kt, products, first, final):
                for half in range(2):
                    last = nc.tensor.matmul(acc2[half * O2:(half + 1) * O2, 0:W // 2], w2_sb[:, kt, :],
                                            products[:, half * (W // 2):(half + 1) * (W // 2)],
                                            start=first, stop=final)
                return last

            def layer2(n, k):
                if not is_first(n, k):
                    pe.wait_ge(second_ready, tile(n, k))
                for b in range(NB):
                    pe.wait_ge(z_made, b_group(n, k, b + 1))
                    for g in range(G):
                        last = contract2(NT + b * G + g, z[:, (LEAD + ahead(n, k) + b) % RING, g, :],
                                         b == 0 and g == 0, b == NB - 1 and g == G - 1)
                    last.then_inc(z_used, 1)
                    if b in (2, 4):
                        p = (b - 2) // 2
                        pe.wait_ge(zp_made, times(n, k, NP, p + 1))
                        for g in range(G):
                            last = contract2(p * G + g, zp[:, p, g, :], False, False)
                        last.then_inc(zp_used, 1)

            def step(n, k):
                layer1(n, k + 1, a_group(n, k + 1, 0), LEAD)
                layer2(n, k)

            pe.wait_ge(w1_ready, 2)
            layer1(0, 0, 0, 0)
            pe.wait_ge(w2_loaded, 32)
            steps(pe, step)
            layer2(LOOPS, 1)


def kernel(r_x, L0_rec_W1, L0_rec_b1, L0_rec_W2, L0_rec_b2):
    import numpy as np
    import concourse.bacc as bacc
    from concourse import mybir
    from concourse.bass_utils import run_bass_kernel_spmd as run

    x = np.asarray(r_x)
    tiles = x.shape[0] // BT
    xt = x.reshape(tiles, BT, F, E).transpose(0, 2, 1, 3).reshape(tiles, F, W)
    row = np.arange(128 + 4 * (NT - 1))
    turned = np.ascontiguousarray(xt[:, (row // 2 + row % 2) % F, :])
    dup = np.ascontiguousarray(xt[:, ((np.arange(160) - 32) // 2) % F, :])

    i, r = np.arange(128) // 2, np.arange(128) % 2
    t = np.arange(NT)
    f = (i[:, None] + 2 * t[None, :] + r[:, None]) % F
    h = (i[:, None] - 16 * np.arange(NC2)[None, :]) % F
    ff = np.broadcast_to(f[:, None, :], (128, NC2, NT)).reshape(128, NC2 * NT)
    hh = np.broadcast_to(h[:, :, None], (128, NC2, NT)).reshape(128, NC2 * NT)
    w2 = np.asarray(L0_rec_W2).reshape(O2, F, F)
    w2 = np.ascontiguousarray(w2[:, ff, hh].transpose(1, 2, 0))
    near = np.arange(128) % 32
    f1 = np.concatenate([ff[:, :NC1 * NT], near[:, None]], axis=1)
    h1 = np.concatenate([hh[:, :NC1 * NT], near[:, None] + 32], axis=1)
    w1 = np.asarray(L0_rec_W1).reshape(O1, F, F)
    w1a = np.ascontiguousarray(w1[:, f1, h1].transpose(1, 2, 0))
    w1b = np.ascontiguousarray(w1[:, h1, f1].transpose(1, 2, 0))
    arrays = {
        "turned": turned, "dup": dup, "w1": w1a, "w1_swapped": w1b, "w2": w2,
        "partner": (np.arange(128) % 2).astype(np.float32).reshape(128, 1),
        "b1": np.asarray(L0_rec_b1).reshape(O1, 1).copy(),
        "b2": np.tile(np.asarray(L0_rec_b2).reshape(O2, 1), (2, 1)),
    }
    nc = bacc.Bacc("TRN2", target_bir_lowering=False, num_devices=1)
    f32 = mybir.dt.float32
    args = [nc.dram_tensor(name, a.shape, f32, kind="ExternalInput").ap() for name, a in arrays.items()]
    out_direct = nc.dram_tensor("out_direct", (O2, tiles, BT), f32, kind="ExternalOutput").ap()
    out_second = nc.dram_tensor("out_second", (2 * O2, tiles, BT // 2), f32, kind="ExternalOutput").ap()
    build(nc, *args, out_direct, out_second)
    result = run(nc, [arrays], core_ids=[0]).results[0]
    direct = result["out_direct"].reshape(O2, tiles * BT)
    second = result["out_second"].reshape(2, O2, tiles, BT // 2).transpose(1, 2, 0, 3).reshape(O2, tiles * BT)
    return np.ascontiguousarray(np.concatenate([direct, second], axis=0).T)
```

```python
import concourse.bass as bass
from concourse import mybir
from contextlib import ExitStack

F = 64
O1, O2 = 128, 64
E = 32
W = 512
BT = W // E
NT = 8
NC1, NC2 = 2, 4
K1 = NC1 * NT
SLOTS = 3

NS = 6
PAIR = 2
X_RING, H_RING, L_RING = 3, 6, 6
G = 4
KW = NS * PAIR
HG = NT // G
NB = (NC2 - 1) * HG
NP = HG
RING = 3
STEP = 1 + NB

PE_1 = [("h", 0), ("h", 1), ("l", 0), ("w", 0), ("l", 1), ("h", 2), ("l", 2), ("h", 3), ("l", 3), ("h", 4),
        ("h", 5), ("l", 4), ("l", 5), ("far", 0)]
PE_2 = [("b", 0), ("b", 1), ("p", 0), ("b", 2), ("b", 3), ("p", 1), ("b", 4), ("b", 5)]
DVE_ORDER = [("x", 3), ("w", 0), ("x", 4), ("b", 0), ("x", 5), ("b", 1), ("b", 2), ("sums", 0),
             ("next x", 0), ("b", 3), ("next x", 1), ("b", 4), ("next x", 2), ("b", 5)]
ACT_ORDER = [("h", 3), ("h", 4), ("take z2", 0), ("h", 5), ("next v", 0), ("take z1", 0), ("next h", 0), ("turn", 1),
             ("next h", 1), ("turn", 2), ("next h", 2), ("turn", 3)]
X_FIRST = 3


def build(nc, turned, dup, w1, w1_swapped, w2, partner, b1, b2, out_direct, out_second):
    f32 = mybir.dt.float32
    f32r = mybir.dt.float32r
    ALU = mybir.AluOpType
    ACT = mybir.ActivationFunctionType
    AX = mybir.AxisListType
    tiles = turned.shape[0]
    LOOPS = (tiles - 2) // SLOTS
    assert 1 + SLOTS * LOOPS == tiles - 1
    assert SLOTS * STEP % RING == 0 and SLOTS * NS % X_RING == 0 and NS % H_RING == 0 and NS % L_RING == 0

    ctx = ExitStack()
    with ctx:
        def sb(name, shape, dtype=f32):
            return ctx.enter_context(nc.sbuf_tensor(name, shape, dtype))

        def pb(name, shape):
            return ctx.enter_context(nc.psum_tensor(name, shape, f32))

        def sem(name):
            return ctx.enter_context(nc.semaphore(name))

        R = sb("R", [128, SLOTS, NT, W])
        V = sb("V", [128, NC1, W])
        far = sb("far", [128, 2, W])
        w1_hi = sb("w1_hi", [128, KW, O1], f32r)
        w1_lo = sb("w1_lo", [128, KW, O1], f32r)
        w1_whole = sb("w1_whole", [128, K1 + 1 - KW, O1])
        w2_sb = sb("w2_sb", [128, NC2 * NT, O2])
        partner_sb = sb("partner_sb", [128, 1])
        b1_sb = sb("b1_sb", [O1, 1])
        b2_sb = sb("b2_sb", [2 * O2, 1])
        x1 = sb("x1", [128, X_RING, PAIR, W])
        x1_hi = sb("x1_hi", [128, H_RING, PAIR, W], f32r)
        x1_lo = sb("x1_lo", [128, L_RING, PAIR, W], f32r)
        z = sb("z", [128, RING, G, W])
        zp = sb("zp", [128, NP, G, W])
        zs = sb("zs", [128, W])
        hid = sb("hid", [128, W])
        Hd = sb("Hd", [128, SLOTS, W])
        direct = sb("direct", [64, W])
        second = sb("second", [128, W // 2])
        sum_direct = sb("sum_direct", [64, tiles, BT])
        sum_second = sb("sum_second", [128, tiles, BT // 2])
        Vp = pb("Vp", [128, NC1, W])
        Hp = pb("Hp", [128, NC2 - 1, W])
        acc1 = pb("acc1", [O1, W])
        acc2 = pb("acc2", [2 * O2, W])

        z_flat = z[:].rearrange("p r g w -> p (r g w)")
        w1_raw = z_flat[:, 0:(K1 + 1) * O1].rearrange("p (k o) -> p k o", o=O1)
        w1_other = z_flat[:, (K1 + 1) * O1:2 * (K1 + 1) * O1].rearrange("p (k o) -> p k o", o=O1)

        w1_loaded = sem("w1_loaded")
        w2_loaded = sem("w2_loaded")
        w1_summed = sem("w1_summed")
        w1_rounded = sem("w1_rounded")
        w1_ready = sem("w1_ready")
        r_loaded = [sem(f"r_loaded{s}") for s in range(SLOTS)]
        far_loaded = [sem(f"far_loaded{s}") for s in range(SLOTS)]
        v_loaded = sem("v_loaded")
        v_ready = sem("v_ready")
        h_ready = sem("h_ready")
        hid_ready = sem("hid_ready")
        hd_loaded = sem("hd_loaded")
        direct_ready = sem("direct_ready")
        second_ready = sem("second_ready")
        direct_summed = sem("direct_summed")
        second_summed = sem("second_summed")
        z_made = sem("z_made")
        z_used = sem("z_used")
        x_made = sem("x_made")
        hi_made = sem("hi_made")
        hi_used = sem("hi_used")
        lo_made = sem("lo_made")
        lo_used = sem("lo_used")
        zp_made = sem("zp_made")
        zp_used = sem("zp_used")
        zs_made = sem("zs_made")
        z1_done = sem("z1_done")
        stored = sem("stored")

        block = ctx.enter_context(nc.Block())

        def times(n, k, count, more=0):
            return n * (SLOTS * count) + (k * count + more)

        def tile(n, k):
            return times(n, k, 1)

        def is_first(n, k):
            return isinstance(n, int) and (n, k) == (0, 0)

        def is_last(n, k):
            return isinstance(n, int) and tile(n, k) == tiles - 1

        def rounds(n, k):
            return n + k // SLOTS + 1

        def w_group(n, k):
            return 0 if is_first(n, k) else times(n, k, STEP, 1 - STEP)

        def b_group(n, k, b):
            return times(n, k, STEP, (1 if is_last(n, k) else 2) + b)

        def buffer(group, k, *more):
            return group(0, k, *more) % RING

        def exists(n, k):
            return not isinstance(n, int) or tile(n, k) < tiles

        def steps(engine, step, loops=LOOPS):
            step(0, 0)
            with engine.Fori(0, loops) as n:
                for k in range(1, 1 + SLOTS):
                    step(n, k)
            for n in range(loops, LOOPS):
                for k in range(1, 1 + SLOTS):
                    step(n, k)

        @block.sync
        def _(sp):
            def load(n, k):
                s = k % SLOTS
                sp.dma_start(far[32 * s:32 * s + 32, :, :],
                             bass.AP(tensor=dup.tensor, offset=times(n, k, 160 * W, 32 * W),
                                     ap=[[2 * W, 32], [64 * W, 2], [1, W]])).then_inc(far_loaded[s], 16)
                sp.dma_start(R[:, s, :, :],
                             bass.AP(tensor=turned.tensor, offset=times(n, k, 156 * W),
                                     ap=[[W, 128], [4 * W, NT], [1, W]])).then_inc(r_loaded[s], 16)

            def reload(n, k):
                sp.wait_ge(z_used, b_group(n, k - SLOTS, NB))
                load(n, k)

            sp.dma_start(w1_raw, w1).then_inc(w1_loaded, 16)
            sp.dma_start(w1_other, w1_swapped).then_inc(w1_loaded, 16)
            sp.dma_start(b1_sb[:], b1).then_inc(w1_loaded, 16)
            sp.dma_start(partner_sb[:], partner).then_inc(w1_loaded, 16)
            load(0, 0)
            load(0, 1)
            sp.dma_start(w2_sb[:], w2).then_inc(w2_loaded, 16)
            sp.dma_start(b2_sb[:], b2).then_inc(w2_loaded, 16)
            load(0, 2)
            loads = (tiles - SLOTS) // SLOTS
            with sp.Fori(1, 1 + loads) as n:
                for k in range(SLOTS):
                    reload(n, k)
            for k in range((tiles - SLOTS) % SLOTS):
                reload(1 + loads, k)
            sp.wait_ge(direct_summed, tiles)
            sp.dma_start(out_direct, sum_direct[:]).then_inc(stored, 16)
            sp.wait_ge(second_summed, tiles)
            sp.dma_start(out_second, sum_second[:]).then_inc(stored, 16)
            sp.wait_ge(stored, 32)

        @block.scalar
        def _(act):
            def load_v(n, k):
                if not is_first(n, k):
                    act.wait_ge(v_ready, tile(n, k))
                act.dma_start(V[:], bass.AP(tensor=dup.tensor, offset=times(n, k, 160 * W),
                                            ap=[[W, 128], [32 * W, NC1], [1, W]])).then_inc(v_loaded, 16)

            def copy_v(n, k):
                act.wait_ge(v_loaded, times(n, k + 1, 16))
                if not is_first(n, k):
                    act.wait_ge(x_made, times(n, k, NS))
                    act.wait_ge(z_made, 1 if isinstance(n, int) and k == 1 else times(n, k - 1, STEP, 2 - STEP))
                nc.scalar.activation(Vp[:], V[:], ACT.Copy).then_inc(v_ready, 1)
                if exists(n, k + 1):
                    load_v(n, k + 1)

            def turn_h(n, k, c):
                if c == 1:
                    act.wait_ge(hd_loaded, times(n, k + 1, 32))
                if not is_first(n, k):
                    act.wait_ge(z_made, b_group(n, k - 1, c * HG))
                size = 64 if c == 2 else 32
                for q in range(0, 128, size):
                    to = (q + 32 * c) % 128
                    last = nc.scalar.activation(Hp[to:to + size, c - 1, :], Hd[q:q + size, k % SLOTS, :], ACT.Copy)
                last.then_inc(h_ready, 1)

            def high_part(n, k, s):
                act.wait_ge(x_made, times(n, k, NS, s + 1))
                if not is_first(n, k):
                    act.wait_ge(hi_used, times(n, k, NS, s + 1 - H_RING))
                nc.scalar.activation(x1_hi[:, s % H_RING, :, :], x1[:, (k * NS + s) % X_RING, :, :],
                                     ACT.Copy).then_inc(hi_made, 1)

            def take_z1(n, k):
                act.wait_ge(z1_done, tile(n, k + 1))
                if not is_first(n, k):
                    act.wait_ge(hd_loaded, times(n, k, 32))
                nc.scalar.activation(hid[64:128, :], acc1[64:128, :], ACT.Relu,
                                     bias=b1_sb[64:128, :]).then_inc(hid_ready, 1)
                act.wait_ge(hid_ready, tile(n, k + 1))
                for r in range(2):
                    act.dma_start(Hd[r::2, k % SLOTS, :], hid[64:128, :]).then_inc(hd_loaded, 16)
                if not is_first(n, k):
                    act.wait_ge(direct_summed, tile(n, k))
                nc.scalar.activation(direct[:], acc1[0:64, :], ACT.Relu,
                                     bias=b1_sb[0:64, :]).then_inc(direct_ready, 1)

            def take_z2(n, k):
                act.wait_ge(z_used, b_group(n, k, NB))
                nc.scalar.activation(second[:], acc2[:, 0:W // 2], ACT.Relu,
                                     bias=b2_sb[:]).then_inc(second_ready, 1)

            def step(n, k):
                for what, number in ACT_ORDER:
                    if what == "h":
                        high_part(n, k + 1, number)
                    if what == "next h" and exists(n, k + 2):
                        high_part(n, k + 2, number)
                    if what == "next v" and exists(n, k + 2):
                        copy_v(n, k + 2)
                    if what == "take z1":
                        take_z1(n, k + 1)
                    if what == "take z2" and not is_first(n, k):
                        take_z2(n, k - 1)
                    if what == "turn":
                        turn_h(n, k + 1, number)

            load_v(0, 0)
            act.wait_ge(w1_summed, 1)
            nc.scalar.activation(w1_hi[:], w1_raw[:, 0:KW, :], ACT.Copy).then_inc(w1_rounded, 1)
            copy_v(0, 0)
            for s in range(NS):
                high_part(0, 0, s)
            copy_v(0, 1)
            take_z1(0, 0)
            for s in range(X_FIRST):
                high_part(0, 1, s)
            for c in range(1, NC2):
                turn_h(0, 0, c)
            act.wait_ge(w2_loaded, 32)
            steps(act, step, LOOPS - 1)
            n, k = LOOPS, 1
            take_z2(n, k - 1)
            act.wait_ge(second_summed, tile(n, k))
            take_z2(n, k)

        @block.vector
        def _(dve):
            def v_copy(c, count):
                return Vp[:, NC1 - 1 - c, :].unsqueeze(1).to_broadcast([128, count, W])

            def split_products(n, k, s):
                if s == 0:
                    dve.wait_ge(v_ready, tile(n, k + 1))
                    dve.wait_ge(r_loaded[k % SLOTS], 16 * rounds(n, k))
                if not is_first(n, k) or s >= X_RING:
                    dve.wait_ge(lo_made, times(n, k, NS, s + 1 - X_RING))
                c, t = divmod(s * PAIR, NT)
                nc.vector.tensor_tensor(x1[:, (k * NS + s) % X_RING, :, :], v_copy(c, PAIR),
                                        R[:, k % SLOTS, t:t + PAIR, :], ALU.mult).then_inc(x_made, 1)

            def whole_products(n, k):
                if not is_first(n, k):
                    free = w_group(n, k) - RING + 1
                    if not isinstance(n, int) or free > 0:
                        dve.wait_ge(z_used, free)
                c, t = divmod(KW, NT)
                nc.vector.tensor_tensor(z[:, buffer(w_group, k), :, :], v_copy(c, G),
                                        R[:, k % SLOTS, t:t + G, :], ALU.mult).then_inc(z_made, 1)

            def layer2_products(n, k, b):
                c, half = divmod(b, HG)
                if half == 0:
                    dve.wait_ge(h_ready, times(n, k, NC2 - 1, c + 1))
                if not is_first(n, k) or b_group(n, k, b) >= RING:
                    dve.wait_ge(z_used, b_group(n, k, b) - RING + 1)
                nc.vector.tensor_tensor(z[:, (b_group(0, k, b) - (1 if is_last(n, k) else 0)) % RING, :, :],
                                        Hp[:, c, :].unsqueeze(1).to_broadcast([128, G, W]),
                                        R[:, k % SLOTS, half * G:(half + 1) * G, :], ALU.mult).then_inc(z_made, 1)

            def sum_z1(n, k):
                dve.wait_ge(direct_ready, tile(n, k + 1))
                nc.vector.tensor_reduce(sum_direct[:, bass.ds(tile(n, k), 1), :].rearrange("p o b -> p (o b)"),
                                        direct[:].rearrange("p (b e) -> p b e", e=E),
                                        AX.X, ALU.add).then_inc(direct_summed, 1)

            def sum_z2(n, k):
                dve.wait_ge(second_ready, tile(n, k + 1))
                nc.vector.tensor_reduce(sum_second[:, bass.ds(tile(n, k), 1), :].rearrange("p o b -> p (o b)"),
                                        second[:].rearrange("p (b e) -> p b e", e=E),
                                        AX.X, ALU.add).then_inc(second_summed, 1)

            def step(n, k):
                for what, number in DVE_ORDER:
                    if what == "x" and not is_last(n, k):
                        split_products(n, k + 1, number)
                    if what == "next x" and exists(n, k + 2):
                        split_products(n, k + 2, number)
                    if what == "w" and not is_last(n, k):
                        whole_products(n, k + 1)
                    if what == "b":
                        layer2_products(n, k, number)
                    if what == "sums":
                        sum_z1(n, k)
                        if not is_first(n, k):
                            sum_z2(n, k - 1)

            dve.wait_ge(w1_loaded, 64)
            nc.vector.scalar_tensor_tensor(out=w1_raw[:, 0, :], in0=w1_other[:, 0, :], scalar=partner_sb[:, 0:1],
                                           in1=w1_raw[:, 0, :], op0=ALU.mult, op1=ALU.add)
            nc.vector.tensor_tensor(w1_raw[:, 1:KW, :], w1_raw[:, 1:KW, :], w1_other[:, 1:KW, :],
                                    ALU.add).then_inc(w1_summed, 1)
            nc.vector.tensor_tensor(w1_whole[:], w1_raw[:, KW:, :], w1_other[:, KW:, :], ALU.add)
            dve.wait_ge(w1_rounded, 1)
            nc.vector.tensor_tensor(w1_lo[:], w1_raw[:, 0:KW, :], w1_hi[:].bitcast(f32),
                                    ALU.subtract).then_inc(w1_ready, 1)
            dve.wait_ge(w1_ready, 1)
            for s in range(X_FIRST):
                split_products(0, 0, s)
            whole_products(0, 0)
            for s in range(X_FIRST, NS):
                split_products(0, 0, s)
            for s in range(X_FIRST):
                split_products(0, 1, s)
            steps(dve, step, LOOPS - 1)
            step(LOOPS, 1)
            sum_z2(LOOPS, 1)

        @block.gpsimd
        def _(pool):
            def far_products(n, k):
                s = k % SLOTS
                pool.wait_ge(far_loaded[s], 16 * rounds(n, k))
                pool.wait_ge(lo_made, times(n, k + 1, NS))
                q = slice(32 * s, 32 * s + 32)
                nc.gpsimd.tensor_tensor(zs[q, :], far[q, 0, :], far[q, 1, :], ALU.mult).then_inc(zs_made, 1)
                pool.wait_ge(zs_made, tile(n, k + 1))

            def low_part(n, k, s):
                pool.wait_ge(hi_made, times(n, k, NS, s + 1))
                if not is_first(n, k):
                    pool.wait_ge(lo_used, times(n, k, NS, s + 1 - L_RING))
                nc.gpsimd.tensor_tensor(x1_lo[:, s % L_RING, :, :], x1[:, (k * NS + s) % X_RING, :, :],
                                        x1_hi[:, s % H_RING, :, :].bitcast(f32), ALU.subtract).then_inc(lo_made, 1)

            def layer2(n, k):
                s = k % SLOTS
                pool.wait_ge(r_loaded[s], 16 * rounds(n, k))
                pool.wait_ge(hd_loaded, times(n, k + 1, 32))
                for g in range(NP):
                    if not is_first(n, k):
                        pool.wait_ge(zp_used, times(n, k - 1, NP, g + 1))
                    nc.gpsimd.tensor_tensor(
                        zp[:, g, :, :], Hd[:, s, :].unsqueeze(1).to_broadcast([128, G, W]),
                        R[:, s, g * G:(g + 1) * G, :], ALU.mult).then_inc(zp_made, 1)

            def layer1(n, k):
                for s in range(NS):
                    low_part(n, k, s)
                far_products(n, k)

            def step(n, k):
                layer1(n, k + 1)
                layer2(n, k)

            layer1(0, 0)
            steps(pool, step)
            layer2(LOOPS, 1)

        @block.tensor
        def _(pe):
            def layer1(n, k):
                if not is_first(n, k):
                    pe.wait_ge(direct_ready, tile(n, k))
                for at, (what, number) in enumerate(PE_1):
                    first, final = at == 0, at == len(PE_1) - 1
                    if what == "h":
                        pe.wait_ge(hi_made, times(n, k, NS, number + 1))
                        for g in range(PAIR):
                            for w1_part in (w1_hi, w1_lo):
                                last = nc.tensor.matmul(acc1[:], w1_part[:, number * PAIR + g, :],
                                                        x1_hi[:, number % H_RING, g, :],
                                                        start=first and g == 0 and w1_part is w1_hi, stop=False)
                        last.then_inc(hi_used, 1)
                    if what == "l":
                        pe.wait_ge(lo_made, times(n, k, NS, number + 1))
                        for g in range(PAIR):
                            last = nc.tensor.matmul(acc1[:], w1_hi[:, number * PAIR + g, :],
                                                    x1_lo[:, number % L_RING, g, :],
                                                    start=False, stop=final and g == PAIR - 1)
                        last.then_inc(lo_used, 1)
                    if what == "w":
                        pe.wait_ge(z_made, 1 if is_first(n, k) else times(n, k, STEP, 2 - STEP))
                        for g in range(G):
                            last = nc.tensor.matmul(acc1[:], w1_whole[:, g, :], z[:, buffer(w_group, k), g, :],
                                                    start=False, stop=False)
                        last.then_inc(z_used, 1)
                    if what == "far":
                        s = k % SLOTS
                        q = slice(32 * s, 32 * s + 32)
                        pe.wait_ge(zs_made, tile(n, k + 1))
                        nc.tensor.matmul(acc1[:], w1_whole[q, G, :], zs[q, :], start=False, stop=final)\
                          .then_inc(z1_done, 1)

            def contract2(kt, products, first, final):
                for half in range(2):
                    last = nc.tensor.matmul(acc2[half * O2:(half + 1) * O2, 0:W // 2], w2_sb[:, kt, :],
                                            products[:, half * (W // 2):(half + 1) * (W // 2)],
                                            start=first, stop=final)
                return last

            def layer2(n, k):
                if not is_first(n, k):
                    pe.wait_ge(second_ready, tile(n, k))
                for at, (what, number) in enumerate(PE_2):
                    first, final = at == 0, at == len(PE_2) - 1
                    if what == "b":
                        pe.wait_ge(z_made, b_group(n, k, number + 1))
                        for g in range(G):
                            last = contract2(NT + number * G + g,
                                             z[:, (b_group(0, k, number) - (1 if is_last(n, k) else 0)) % RING, g, :],
                                             first and g == 0, final and g == G - 1)
                        last.then_inc(z_used, 1)
                    if what == "p":
                        pe.wait_ge(zp_made, times(n, k, NP, number + 1))
                        for g in range(G):
                            last = contract2(number * G + g, zp[:, number, g, :], False, False)
                        last.then_inc(zp_used, 1)

            def step(n, k):
                layer1(n, k + 1)
                layer2(n, k)

            pe.wait_ge(w1_ready, 1)
            layer1(0, 0)
            pe.wait_ge(w2_loaded, 32)
            steps(pe, step)
            layer2(LOOPS, 1)


def kernel(r_x, L0_rec_W1, L0_rec_b1, L0_rec_W2, L0_rec_b2):
    import numpy as np
    import concourse.bacc as bacc
    from concourse import mybir
    from concourse.bass_utils import run_bass_kernel_spmd as run

    x = np.asarray(r_x)
    tiles = x.shape[0] // BT
    xt = x.reshape(tiles, BT, F, E).transpose(0, 2, 1, 3).reshape(tiles, F, W)
    row = np.arange(128 + 4 * (NT - 1))
    turned = np.ascontiguousarray(xt[:, (row // 2 + row % 2) % F, :])
    dup = np.ascontiguousarray(xt[:, ((np.arange(160) - 32) // 2) % F, :])

    i, r = np.arange(128) // 2, np.arange(128) % 2
    t = np.arange(NT)
    f = (i[:, None] + 2 * t[None, :] + r[:, None]) % F
    h = (i[:, None] - 16 * np.arange(NC2)[None, :]) % F
    ff = np.broadcast_to(f[:, None, :], (128, NC2, NT)).reshape(128, NC2 * NT)
    hh = np.broadcast_to(h[:, :, None], (128, NC2, NT)).reshape(128, NC2 * NT)
    w2 = np.asarray(L0_rec_W2).reshape(O2, F, F)
    w2 = np.ascontiguousarray(w2[:, ff, hh].transpose(1, 2, 0))
    near = np.arange(128) % 32
    f1 = np.concatenate([ff[:, :NC1 * NT], near[:, None]], axis=1)
    h1 = np.concatenate([hh[:, :NC1 * NT], near[:, None] + 32], axis=1)
    w1 = np.asarray(L0_rec_W1).reshape(O1, F, F)
    w1a = np.ascontiguousarray(w1[:, f1, h1].transpose(1, 2, 0))
    w1b = np.ascontiguousarray(w1[:, h1, f1].transpose(1, 2, 0))
    arrays = {
        "turned": turned, "dup": dup, "w1": w1a, "w1_swapped": w1b, "w2": w2,
        "partner": (np.arange(128) % 2).astype(np.float32).reshape(128, 1),
        "b1": np.asarray(L0_rec_b1).reshape(O1, 1).copy(),
        "b2": np.tile(np.asarray(L0_rec_b2).reshape(O2, 1), (2, 1)),
    }
    nc = bacc.Bacc("TRN2", target_bir_lowering=False, num_devices=1)
    f32 = mybir.dt.float32
    args = [nc.dram_tensor(name, a.shape, f32, kind="ExternalInput").ap() for name, a in arrays.items()]
    out_direct = nc.dram_tensor("out_direct", (O2, tiles, BT), f32, kind="ExternalOutput").ap()
    out_second = nc.dram_tensor("out_second", (2 * O2, tiles, BT // 2), f32, kind="ExternalOutput").ap()
    build(nc, *args, out_direct, out_second)
    result = run(nc, [arrays], core_ids=[0]).results[0]
    direct = result["out_direct"].reshape(O2, tiles * BT)
    second = result["out_second"].reshape(2, O2, tiles, BT // 2).transpose(1, 2, 0, 3).reshape(O2, tiles * BT)
    return np.ascontiguousarray(np.concatenate([direct, second], axis=0).T)
```

```python
import concourse.bass as bass
from concourse import mybir
from contextlib import ExitStack

F = 64
O1, O2 = 128, 64
E = 32
W = 512
BT = W // E
NT = 8
NC1, NC2 = 2, 4
K1 = NC1 * NT
R_ROWS = 128 + 4 * (NT - 1)
V_ROWS = 128 + 32 * (NC1 - 1)
SLOTS = 3

NS = 7
PAIR = 2
X_RING = 3
PART_BUFFER = [0, 1, 2, 3, 4, 5, 2]
KW = NS * PAIR
GW = K1 - KW
G = 4
HG = NT // G
NB = (NC2 - 1) * HG
NP = HG
RING = 3
STEP = 1 + NB

PE_1 = [("h", 0), ("h", 1), ("l", 0), ("w", 0), ("l", 1), ("h", 2), ("l", 2), ("h", 3), ("l", 3), ("h", 4),
        ("l", 4), ("h", 5), ("l", 5), ("h", 6), ("l", 6), ("far", 0)]
PE_FIRST = [("h", 0), ("h", 1), ("l", 0), ("l", 1), ("h", 2), ("h", 3), ("l", 2), ("l", 3), ("h", 4), ("h", 5),
            ("l", 4), ("w", 0), ("l", 5), ("h", 6), ("l", 6), ("far", 0)]
PE_2 = [("b", 0), ("b", 1), ("p", 0), ("b", 2), ("b", 3), ("p", 1), ("b", 4), ("b", 5)]
DVE_ORDER = [("x", 3), ("w", 0), ("x", 4), ("x", 5), ("b", 0), ("x", 6), ("b", 1), ("join", 0), ("b", 2),
             ("sums", 0), ("next x", 0), ("next far", 0), ("b", 3), ("next x", 1), ("next far low", 0),
             ("b", 4), ("next x", 2), ("b", 5)]
ACT_ORDER = [("h", 3), ("h", 4), ("h", 5), ("take z2", 0), ("h", 6), ("next v", 0), ("relu z2", 0),
             ("take z1", 0), ("next h", 0), ("next far", 0), ("load v", 0), ("turn", 1), ("next h", 1),
             ("turn", 2), ("next h", 2), ("turn", 3)]
X_FIRST = 3
W1_PARTS = [(0, 2), (2, 6), (6, KW), (KW, K1 + 1)]
R_PARTS = [(0, 2), (2, 4), (4, NT)]


def build(nc, turned, dup, w1, w1_swapped, w2, parity, b1, b2, out_direct, out_second):
    f32 = mybir.dt.float32
    f32r = mybir.dt.float32r
    ALU = mybir.AluOpType
    ACT = mybir.ActivationFunctionType
    AX = mybir.AxisListType
    tiles = turned.shape[0]
    LOOPS = (tiles - 2) // SLOTS
    assert 1 + SLOTS * LOOPS == tiles - 1
    assert SLOTS * STEP % RING == 0 and SLOTS * NS % X_RING == 0

    ctx = ExitStack()
    with ctx:
        def sb(name, shape, dtype=f32):
            return ctx.enter_context(nc.sbuf_tensor(name, shape, dtype))

        def pb(name, shape):
            return ctx.enter_context(nc.psum_tensor(name, shape, f32))

        def sem(name):
            return ctx.enter_context(nc.semaphore(name))

        R = sb("R", [128, SLOTS, NT, W])
        V = sb("V", [128, NC1, W])
        w1_hi = sb("w1_hi", [128, KW, O1], f32r)
        w1_lo = sb("w1_lo", [128, KW, O1], f32r)
        w1_whole = sb("w1_whole", [128, K1 + 1 - KW, O1])
        w1_far_hi = sb("w1_far_hi", [64, O1], f32r)
        w1_far_r = sb("w1_far_r", [64, O1])
        w1_far = sb("w1_far", [64, O1], f32r)
        w2_sb = sb("w2_sb", [128, NC2 * NT, O2])
        parity_sb = sb("parity_sb", [128, 2])
        b1_sb = sb("b1_sb", [O1, 1])
        b2_sb = sb("b2_sb", [2 * O2, 1])
        x1 = sb("x1", [128, X_RING, PAIR, W])
        x1_hi = sb("x1_hi", [128, max(PART_BUFFER) + 1, PAIR, W], f32r)
        x1_lo = sb("x1_lo", [128, max(PART_BUFFER) + 1, PAIR, W], f32r)
        z = sb("z", [128, RING, G, W])
        zp = sb("zp", [128, NP, G, W])
        far_hi = sb("far_hi", [64, W], f32r)
        far_lo = sb("far_lo", [64, W], f32r)
        hid = sb("hid", [128, W])
        Hd = sb("Hd", [128, SLOTS, W])
        low_half = sb("low_half", [128, W])
        joined = sb("joined", [128, W])
        rows = sb("rows", [128, W])
        sums = sb("sums", [128, tiles + 1, BT])
        Vp = pb("Vp", [128, NC1, W])
        Hp = pb("Hp", [128, NC2 - 1, W])
        far = pb("far", [64, W])
        acc1 = pb("acc1", [O1, W])
        acc2 = pb("acc2", [2 * O2, W])

        z_flat = z[:].rearrange("p r g w -> p (r g w)")
        w1_raw = z_flat[:, 0:(K1 + 1) * O1].rearrange("p (k o) -> p k o", o=O1)
        w1_other = z_flat[:, (K1 + 1) * O1:2 * (K1 + 1) * O1].rearrange("p (k o) -> p k o", o=O1)

        b1_loaded = sem("b1_loaded")
        w1_loaded = [sem(f"w1_loaded{i}") for i in range(len(W1_PARTS))]
        w2_loaded = sem("w2_loaded")
        w1_summed = sem("w1_summed")
        w1_rounded = sem("w1_rounded")
        w1_ready = sem("w1_ready")
        r_loaded = [sem(f"r_loaded{s}") for s in range(SLOTS)]
        first_loaded = [sem(f"first_loaded{i}") for i in range(len(R_PARTS) - 1)] + [r_loaded[0]]
        v_loaded = sem("v_loaded")
        v_ready = sem("v_ready")
        h_ready = sem("h_ready")
        hid_ready = sem("hid_ready")
        hd_loaded = sem("hd_loaded")
        direct_ready = sem("direct_ready")
        low_half_ready = sem("low_half_ready")
        joined_ready = sem("joined_ready")
        second_ready = sem("second_ready")
        rows_summed = sem("rows_summed")
        far_made = sem("far_made")
        far_hi_made = sem("far_hi_made")
        far_lo_made = sem("far_lo_made")
        w1_far_ready = sem("w1_far_ready")
        z_made = sem("z_made")
        z_used = sem("z_used")
        x_made = sem("x_made")
        hi_made = sem("hi_made")
        hi_used = sem("hi_used")
        lo_made = sem("lo_made")
        lo_used = sem("lo_used")
        zp_made = sem("zp_made")
        zp_used = sem("zp_used")
        z1_done = sem("z1_done")
        stored = sem("stored")

        block = ctx.enter_context(nc.Block())

        def times(n, k, count, more=0):
            return n * (SLOTS * count) + (k * count + more)

        def tile(n, k):
            return times(n, k, 1)

        def is_first(n, k):
            return isinstance(n, int) and (n, k) == (0, 0)

        def is_last(n, k):
            return isinstance(n, int) and tile(n, k) == tiles - 1

        def rounds(n, k):
            return n + k // SLOTS + 1

        def w_group(n, k):
            return 0 if is_first(n, k) else times(n, k, STEP, 1 - STEP)

        def b_group(n, k, b):
            return times(n, k, STEP, (1 if is_last(n, k) else 2) + b)

        def w_buffer(n, k):
            return w_group(0, k) % RING

        def b_buffer(n, k, b):
            return (b_group(0, k, b) - (1 if is_last(n, k) else 0)) % RING

        def freed(n, k, s):
            before = [i for i in range(s - NS, s) if PART_BUFFER[i % NS] == PART_BUFFER[s]][-1]
            return 0 if is_first(n, k) and before < 0 else times(n, k, NS, before + 1)

        def z2_sum(n, k):
            return acc1 if is_last(n, k) else acc2

        def columns(half, count=W):
            return slice(0, count) if half is None else slice(half * count // 2, (half + 1) * count // 2)

        def exists(n, k):
            return not isinstance(n, int) or tile(n, k) < tiles

        def steps(engine, step, loops=LOOPS):
            step(0, 0)
            with engine.Fori(0, loops) as n:
                for k in range(1, 1 + SLOTS):
                    step(n, k)
            for n in range(loops, LOOPS):
                for k in range(1, 1 + SLOTS):
                    step(n, k)

        @block.sync
        def _(sp):
            def load(n, k):
                s = k % SLOTS
                sp.dma_start(R[:, s, :, :],
                             bass.AP(tensor=turned.tensor, offset=times(n, k, R_ROWS * W),
                                     ap=[[W, 128], [4 * W, NT], [1, W]])).then_inc(r_loaded[s], 16)

            def reload(n, k):
                sp.wait_ge(z_used, b_group(n, k - SLOTS, NB))
                load(n, k)

            def load_w1(part):
                first, end = W1_PARTS[part]
                for raw, source in ((w1_raw, w1), (w1_other, w1_swapped)):
                    sp.dma_start(raw[:, first:end, :], source[:, first:end, :]).then_inc(w1_loaded[part], 16)

            def load_first(part):
                t, end = R_PARTS[part]
                sp.dma_start(R[:, 0, t:end, :],
                             bass.AP(tensor=turned.tensor, offset=4 * t * W,
                                     ap=[[W, 128], [4 * W, end - t], [1, W]])).then_inc(first_loaded[part], 16)

            sp.dma_start(parity_sb[:], parity).then_inc(w1_loaded[0], 16)
            load_w1(0)
            load_first(0)
            load_first(1)
            load_w1(1)
            load_first(2)
            load_w1(2)
            load_w1(3)
            sp.dma_start(b1_sb[:], b1).then_inc(b1_loaded, 16)
            sp.wait_ge(hi_made, 3)
            load(0, 1)
            sp.dma_start(w2_sb[:], w2).then_inc(w2_loaded, 16)
            sp.dma_start(b2_sb[:], b2).then_inc(w2_loaded, 16)
            load(0, 2)
            loads = (tiles - SLOTS) // SLOTS
            with sp.Fori(1, 1 + loads) as n:
                for k in range(SLOTS):
                    reload(n, k)
            for k in range((tiles - SLOTS) % SLOTS):
                reload(1 + loads, k)
            sp.wait_ge(rows_summed, tiles)
            sp.dma_start(out_direct, sums[0:64, 0:tiles, :]).then_inc(stored, 16)
            sp.dma_start(out_second[:, 0:tiles - 1, :], sums[64:128, 1:tiles, :]).then_inc(stored, 16)
            sp.wait_ge(rows_summed, tiles + 2)
            sp.dma_start(out_second[:, tiles - 1:, :], sums[64:128, tiles:, :]).then_inc(stored, 16)
            sp.wait_ge(stored, 48)

        @block.scalar
        def _(act):
            def load_v(n, k):
                if not is_first(n, k):
                    act.wait_ge(v_ready, tile(n, k))
                    act.wait_ge(far_made, tile(n, k))
                act.dma_start(V[:], bass.AP(tensor=dup.tensor, offset=times(n, k, V_ROWS * W),
                                            ap=[[W, 128], [32 * W, NC1], [1, W]])).then_inc(v_loaded, 16)

            def copy_v(n, k):
                act.wait_ge(v_loaded, times(n, k + 1, 16))
                if not is_first(n, k):
                    act.wait_ge(x_made, times(n, k, NS))
                    act.wait_ge(z_made, 1 if isinstance(n, int) and tile(n, k) == 1 else w_group(n, k - 1) + 1)
                nc.scalar.activation(Vp[:], V[:], ACT.Copy).then_inc(v_ready, 1)

            def turn_h(n, k, c):
                if c == 1:
                    act.wait_ge(hd_loaded, times(n, k + 1, 32))
                if not is_first(n, k):
                    act.wait_ge(z_made, b_group(n, k - 1, c * HG))
                size = 64 if c == 2 else 32
                for q in range(0, 128, size):
                    to = (q + 32 * c) % 128
                    last = nc.scalar.activation(Hp[to:to + size, c - 1, :], Hd[q:q + size, k % SLOTS, :], ACT.Copy)
                last.then_inc(h_ready, 1)

            def high_part(n, k, s):
                act.wait_ge(x_made, times(n, k, NS, s + 1))
                free = freed(n, k, s)
                if not isinstance(free, int) or free > 0:
                    act.wait_ge(hi_used, free)
                nc.scalar.activation(x1_hi[:, PART_BUFFER[s], :, :], x1[:, (k * NS + s) % X_RING, :, :],
                                     ACT.Copy).then_inc(hi_made, 1)

            def take_z1(n, k):
                act.wait_ge(z1_done, tile(n, k + 1))
                if not is_first(n, k):
                    act.wait_ge(hd_loaded, times(n, k, 32))
                nc.scalar.activation(hid[64:128, :], acc1[64:128, :], ACT.Relu,
                                     bias=b1_sb[64:128, :]).then_inc(hid_ready, 1)
                if not is_first(n, k):
                    act.wait_ge(rows_summed, tile(n, k))
                nc.scalar.activation(rows[0:64, :], acc1[0:64, :], ACT.Relu,
                                     bias=b1_sb[0:64, :]).then_inc(direct_ready, 1)
                act.wait_ge(hid_ready, tile(n, k + 1))
                for r in range(2):
                    act.dma_start(Hd[r::2, k % SLOTS, :], hid[64:128, :]).then_inc(hd_loaded, 16)

            def far_high_part(n, k):
                act.wait_ge(far_made, tile(n, k + 1))
                if not is_first(n, k):
                    act.wait_ge(z1_done, tile(n, k))
                nc.scalar.activation(far_hi[:], far[:], ACT.Copy).then_inc(far_hi_made, 1)

            def take_z2(n, k, half=None):
                act.wait_ge(z_used, b_group(n, k, NB))
                some = columns(half)
                nc.scalar.activation(low_half[64:128, some], z2_sum(n, k)[0:64, some],
                                     ACT.Copy).then_inc(low_half_ready, 1)

            def relu_z2(n, k, half=None):
                some = columns(half)
                act.wait_ge(joined_ready, times(n, k, 1, 1 + (half or 0)))
                act.wait_ge(rows_summed, tile(n, k + 1))
                nc.scalar.activation(rows[64:128, some], joined[64:128, some], ACT.Relu,
                                     bias=b2_sb[64:128, :]).then_inc(second_ready, 1)

            def step(n, k):
                for what, number in ACT_ORDER:
                    if what == "h" and not is_first(n, k):
                        high_part(n, k + 1, number)
                    if what == "next h" and exists(n, k + 2):
                        high_part(n, k + 2, number)
                    if what == "next v" and exists(n, k + 2):
                        copy_v(n, k + 2)
                    if what == "take z1":
                        take_z1(n, k + 1)
                    if what == "load v" and exists(n, k + 3):
                        load_v(n, k + 3)
                    if what == "next far" and exists(n, k + 2):
                        far_high_part(n, k + 2)
                    if what == "take z2" and not is_first(n, k):
                        take_z2(n, k - 1)
                    if what == "relu z2" and not is_first(n, k):
                        relu_z2(n, k - 1)
                    if what == "turn":
                        turn_h(n, k + 1, number)

            def round_w1(part):
                act.wait_ge(w1_summed, part + 1)
                if part == len(W1_PARTS) - 1:
                    nc.scalar.activation(w1_far_hi[:], w1_whole[0:64, K1 - KW, :], ACT.Copy).then_inc(w1_rounded, 1)
                else:
                    some = slice(*W1_PARTS[part])
                    nc.scalar.activation(w1_hi[:, some, :], w1_raw[:, some, :], ACT.Copy).then_inc(w1_rounded, 1)

            load_v(0, 0)
            copy_v(0, 0)
            round_w1(0)
            high_part(0, 0, 0)
            high_part(0, 0, 1)
            load_v(0, 1)
            round_w1(1)
            high_part(0, 0, 2)
            high_part(0, 0, 3)
            high_part(0, 0, 4)
            round_w1(2)
            round_w1(3)
            high_part(0, 0, 5)
            high_part(0, 0, 6)
            far_high_part(0, 0)
            copy_v(0, 1)
            for s in range(X_FIRST):
                high_part(0, 1, s)
            act.wait_ge(b1_loaded, 16)
            take_z1(0, 0)
            high_part(0, 1, 3)
            high_part(0, 1, 4)
            high_part(0, 1, 5)
            far_high_part(0, 1)
            turn_h(0, 0, 1)
            load_v(0, 2)
            high_part(0, 1, 6)
            turn_h(0, 0, 2)
            turn_h(0, 0, 3)
            act.wait_ge(w2_loaded, 32)
            steps(act, step, LOOPS - 1)
            n, k = LOOPS, 1
            take_z2(n, k - 1)
            relu_z2(n, k - 1)
            for half in range(2):
                take_z2(n, k, half)
            for half in range(2):
                relu_z2(n, k, half)

        @block.vector
        def _(dve):
            def v_copy(c, count):
                return Vp[:, NC1 - 1 - c, :].unsqueeze(1).to_broadcast([128, count, W])

            def split_products(n, k, s):
                if s == 0:
                    dve.wait_ge(v_ready, tile(n, k + 1))
                if is_first(n, k) and s * PAIR in (0, 2, 4):
                    dve.wait_ge(first_loaded[s], 16)
                elif not is_first(n, k) and s == 0:
                    dve.wait_ge(r_loaded[k % SLOTS], 16 * rounds(n, k))
                if not is_first(n, k) or s >= X_RING:
                    dve.wait_ge(lo_made, times(n, k, NS, s + 1 - X_RING))
                c, t = divmod(s * PAIR, NT)
                nc.vector.tensor_tensor(x1[:, (k * NS + s) % X_RING, :, :], v_copy(c, PAIR),
                                        R[:, k % SLOTS, t:t + PAIR, :], ALU.mult).then_inc(x_made, 1)

            def whole_products(n, k):
                if not is_first(n, k):
                    free = w_group(n, k) - RING + 1
                    if not isinstance(n, int) or free > 0:
                        dve.wait_ge(z_used, free)
                c, t = divmod(KW, NT)
                nc.vector.tensor_tensor(z[:, w_buffer(n, k), 0:GW, :], v_copy(c, GW),
                                        R[:, k % SLOTS, t:t + GW, :], ALU.mult).then_inc(z_made, 1)

            def layer2_products(n, k, b):
                c, half = divmod(b, HG)
                if half == 0:
                    dve.wait_ge(h_ready, times(n, k, NC2 - 1, c + 1))
                if not is_first(n, k) or b_group(n, k, b) >= RING:
                    dve.wait_ge(z_used, b_group(n, k, b) - RING + 1)
                nc.vector.tensor_tensor(z[:, b_buffer(n, k, b), :, :],
                                        Hp[:, c, :].unsqueeze(1).to_broadcast([128, G, W]),
                                        R[:, k % SLOTS, half * G:(half + 1) * G, :], ALU.mult).then_inc(z_made, 1)

            def far_products(n, k):
                if not is_first(n, k):
                    dve.wait_ge(far_lo_made, tile(n, k))
                nc.vector.tensor_tensor(far[:], Vp[0:64, NC1 - 1, :], V[64:128, NC1 - 1, :],
                                        ALU.mult).then_inc(far_made, 1)

            def far_low_part(n, k):
                dve.wait_ge(far_hi_made, tile(n, k + 1))
                nc.vector.tensor_tensor(far_lo[:], far[:], far_hi[:].bitcast(f32),
                                        ALU.subtract).then_inc(far_lo_made, 1)

            def join_z2(n, k, half=None):
                some = columns(half)
                dve.wait_ge(low_half_ready, times(n, k, 1, 1 + (half or 0)))
                if not is_first(n, k):
                    dve.wait_ge(second_ready, tile(n, k))
                nc.vector.tensor_tensor(joined[64:128, some], z2_sum(n, k)[64:128, some], low_half[64:128, some],
                                        ALU.add).then_inc(joined_ready, 1)

            def sum_rows(n, k, part, half=None):
                batch = columns(half, BT)
                nc.vector.tensor_reduce(sums[part, bass.ds(tile(n, k), 1), batch].rearrange("p o b -> p (o b)"),
                                        rows[part, columns(half)].rearrange("p (b e) -> p b e", e=E),
                                        AX.X, ALU.add).then_inc(rows_summed, 1)

            def step(n, k):
                for what, number in DVE_ORDER:
                    if is_first(n, k) and what in ("x", "w"):
                        continue
                    if what == "x" and not is_last(n, k):
                        split_products(n, k + 1, number)
                    if what == "next x" and exists(n, k + 2):
                        split_products(n, k + 2, number)
                    if what == "w" and not is_last(n, k):
                        whole_products(n, k + 1)
                    if what == "b":
                        layer2_products(n, k, number)
                    if what == "next far" and exists(n, k + 2):
                        far_products(n, k + 2)
                    if what == "next far low" and exists(n, k + 2):
                        far_low_part(n, k + 2)
                    if what == "join" and not is_first(n, k):
                        join_z2(n, k - 1)
                    if what == "sums":
                        dve.wait_ge(direct_ready, tile(n, k + 1))
                        if not is_first(n, k):
                            dve.wait_ge(second_ready, tile(n, k))
                        sum_rows(n, k, slice(0, 64 if is_first(n, k) else 128))

            def sum_w1(part):
                first, end = W1_PARTS[part]
                dve.wait_ge(w1_loaded[part], 48 if part == 0 else 32)
                if part == 0:
                    nc.vector.scalar_tensor_tensor(out=w1_raw[:, 0, :], in0=w1_other[:, 0, :],
                                                   scalar=parity_sb[:, 0:1], in1=w1_raw[:, 0, :],
                                                   op0=ALU.mult, op1=ALU.add)
                    first = 1
                to = w1_whole[:] if part == len(W1_PARTS) - 1 else w1_raw[:, first:end, :]
                nc.vector.tensor_tensor(to, w1_raw[:, first:end, :], w1_other[:, first:end, :],
                                        ALU.add).then_inc(w1_summed, 1)

            def low_w1(part):
                dve.wait_ge(w1_rounded, part + 1)
                dve.wait_ge(w1_summed, part + 1)
                some = slice(*W1_PARTS[part])
                nc.vector.tensor_tensor(w1_lo[:, some, :], w1_raw[:, some, :], w1_hi[:, some, :].bitcast(f32),
                                        ALU.subtract).then_inc(w1_ready, 1)

            sum_w1(0)
            split_products(0, 0, 0)
            low_w1(0)
            split_products(0, 0, 1)
            far_products(0, 0)
            sum_w1(1)
            low_w1(1)
            split_products(0, 0, 2)
            split_products(0, 0, 3)
            split_products(0, 0, 4)
            sum_w1(2)
            low_w1(2)
            sum_w1(3)
            dve.wait_ge(w1_summed, len(W1_PARTS))
            dve.wait_ge(w1_ready, len(W1_PARTS) - 1)
            split_products(0, 0, 5)
            split_products(0, 0, 6)
            whole_products(0, 0)
            nc.vector.tensor_scalar(w1_far_r[:], w1_whole[0:64, K1 - KW, :], parity_sb[0:64, 0:1], None,
                                    ALU.mult).then_inc(w1_far_ready, 1)
            dve.wait_ge(w1_rounded, len(W1_PARTS))
            dve.wait_ge(w1_far_ready, 1)
            nc.vector.scalar_tensor_tensor(out=w1_far[:], in0=w1_far_hi[:].bitcast(f32),
                                           scalar=parity_sb[0:64, 1:2], in1=w1_far_r[:],
                                           op0=ALU.mult, op1=ALU.add).then_inc(w1_far_ready, 1)
            split_products(0, 1, 0)
            far_low_part(0, 0)
            for s in range(1, X_FIRST):
                split_products(0, 1, s)
            far_products(0, 1)
            split_products(0, 1, 3)
            whole_products(0, 1)
            for s in range(4, NS):
                split_products(0, 1, s)
            far_low_part(0, 1)
            steps(dve, step, LOOPS - 1)
            step(LOOPS, 1)
            for half in range(2):
                join_z2(LOOPS, 1, half)
            for half in range(2):
                dve.wait_ge(second_ready, tiles + half)
                sum_rows(LOOPS, 2, slice(64, 128), half)

        @block.gpsimd
        def _(pool):
            def low_part(n, k, s):
                pool.wait_ge(hi_made, times(n, k, NS, s + 1))
                free = freed(n, k, s)
                if not isinstance(free, int) or free > 0:
                    pool.wait_ge(lo_used, free)
                nc.gpsimd.tensor_tensor(x1_lo[:, PART_BUFFER[s], :, :], x1[:, (k * NS + s) % X_RING, :, :],
                                        x1_hi[:, PART_BUFFER[s], :, :].bitcast(f32), ALU.subtract).then_inc(lo_made, 1)

            def layer2(n, k):
                s = k % SLOTS
                pool.wait_ge(r_loaded[s], 16 * rounds(n, k))
                pool.wait_ge(hd_loaded, times(n, k + 1, 32))
                for g in range(NP):
                    if not is_first(n, k):
                        pool.wait_ge(zp_used, times(n, k - 1, NP, g + 1))
                    nc.gpsimd.tensor_tensor(
                        zp[:, g, :, :], Hd[:, s, :].unsqueeze(1).to_broadcast([128, G, W]),
                        R[:, s, g * G:(g + 1) * G, :], ALU.mult).then_inc(zp_made, 1)

            def layer1(n, k):
                for s in range(NS):
                    low_part(n, k, s)

            def step(n, k):
                layer1(n, k + 1)
                layer2(n, k)

            layer1(0, 0)
            steps(pool, step)
            layer2(LOOPS, 1)

        @block.tensor
        def _(pe):
            def layer1(n, k):
                if not is_first(n, k):
                    pe.wait_ge(direct_ready, tile(n, k))
                order = PE_FIRST if is_first(n, k) else PE_1
                for at, (what, number) in enumerate(order):
                    first, final = at == 0, at == len(order) - 1
                    if what == "h":
                        if is_first(n, k):
                            pe.wait_ge(w1_ready, [number * PAIR < end for _, end in W1_PARTS].index(True) + 1)
                        pe.wait_ge(hi_made, times(n, k, NS, number + 1))
                        for g in range(PAIR):
                            for w1_part in (w1_hi, w1_lo):
                                last = nc.tensor.matmul(acc1[:], w1_part[:, number * PAIR + g, :],
                                                        x1_hi[:, PART_BUFFER[number], g, :],
                                                        start=first and g == 0 and w1_part is w1_hi, stop=False)
                        last.then_inc(hi_used, 1)
                    if what == "l":
                        pe.wait_ge(lo_made, times(n, k, NS, number + 1))
                        for g in range(PAIR):
                            last = nc.tensor.matmul(acc1[:], w1_hi[:, number * PAIR + g, :],
                                                    x1_lo[:, PART_BUFFER[number], g, :],
                                                    start=False, stop=final and g == PAIR - 1)
                        last.then_inc(lo_used, 1)
                    if what == "w":
                        if is_first(n, k):
                            pe.wait_ge(w1_summed, len(W1_PARTS))
                        pe.wait_ge(z_made, 1 if is_first(n, k) else times(n, k, STEP, 2 - STEP))
                        for g in range(GW):
                            last = nc.tensor.matmul(acc1[:], w1_whole[:, g, :], z[:, w_buffer(n, k), g, :],
                                                    start=False, stop=False)
                        last.then_inc(z_used, 1)
                    if what == "far":
                        pe.wait_ge(far_lo_made, tile(n, k + 1))
                        if is_first(n, k):
                            pe.wait_ge(w1_far_ready, 2)
                        nc.tensor.matmul(acc1[:], w1_far[:], far_hi[:], start=False, stop=False)
                        nc.tensor.matmul(acc1[:], w1_far[:], far_lo[:], start=False, stop=final).then_inc(z1_done, 1)

            def contract2(acc, kt, g, products, first, final):
                half = g % 2
                return nc.tensor.matmul(acc[half * O2:(half + 1) * O2, :], w2_sb[:, kt + g, :], products[:, g, :],
                                        start=first and g < 2, stop=final and g >= G - 2)

            def layer2(n, k):
                acc = z2_sum(n, k)
                if is_last(n, k):
                    pe.wait_ge(direct_ready, tiles)
                elif not is_first(n, k):
                    pe.wait_ge(joined_ready, tile(n, k))
                for at, (what, number) in enumerate(PE_2):
                    first, final = at == 0, at == len(PE_2) - 1
                    if what == "b":
                        pe.wait_ge(z_made, b_group(n, k, number + 1))
                        for g in range(G):
                            last = contract2(acc, NT + number * G, g,
                                             z[:, b_buffer(n, k, number), :, :], first, final)
                        last.then_inc(z_used, 1)
                    if what == "p":
                        pe.wait_ge(zp_made, times(n, k, NP, number + 1))
                        for g in range(G):
                            last = contract2(acc, number * G, g, zp[:, number, :, :], False, False)
                        last.then_inc(zp_used, 1)

            def step(n, k):
                layer1(n, k + 1)
                layer2(n, k)

            layer1(0, 0)
            pe.wait_ge(w2_loaded, 32)
            steps(pe, step)
            layer2(LOOPS, 1)


def kernel(r_x, L0_rec_W1, L0_rec_b1, L0_rec_W2, L0_rec_b2):
    import numpy as np
    import concourse.bacc as bacc
    from concourse import mybir
    from concourse.bass_utils import run_bass_kernel_spmd as run

    x = np.asarray(r_x)
    tiles = x.shape[0] // BT
    xt = x.reshape(tiles, BT, F, E).transpose(0, 2, 1, 3).reshape(tiles, F, W)
    row = np.arange(R_ROWS)
    turned = np.ascontiguousarray(xt[:, (row // 2 + row % 2) % F, :])
    dup = np.ascontiguousarray(xt[:, ((np.arange(V_ROWS) - 32) // 2) % F, :])

    i, r = np.arange(128) // 2, np.arange(128) % 2
    t = np.arange(NT)
    f = (i[:, None] + 2 * t[None, :] + r[:, None]) % F
    h = (i[:, None] - 16 * np.arange(NC2)[None, :]) % F
    ff = np.broadcast_to(f[:, None, :], (128, NC2, NT)).reshape(128, NC2 * NT)
    hh = np.broadcast_to(h[:, :, None], (128, NC2, NT)).reshape(128, NC2 * NT)
    w2 = np.asarray(L0_rec_W2).reshape(O2, F, F)
    w2 = np.ascontiguousarray(w2[:, ff, hh].transpose(1, 2, 0))
    near = i % 32
    f1 = np.concatenate([ff[:, :NC1 * NT], near[:, None]], axis=1)
    h1 = np.concatenate([hh[:, :NC1 * NT], near[:, None] + 32], axis=1)
    w1 = np.asarray(L0_rec_W1).reshape(O1, F, F)
    w1a = np.ascontiguousarray(w1[:, f1, h1].transpose(1, 2, 0))
    w1b = np.ascontiguousarray(w1[:, h1, f1].transpose(1, 2, 0))
    arrays = {
        "turned": turned, "dup": dup, "w1": w1a, "w1_swapped": w1b, "w2": w2,
        "parity": np.stack([r, 1 - 2 * r], axis=1).astype(np.float32),
        "b1": np.asarray(L0_rec_b1).reshape(O1, 1).copy(),
        "b2": np.tile(np.asarray(L0_rec_b2).reshape(O2, 1), (2, 1)),
    }
    nc = bacc.Bacc("TRN2", target_bir_lowering=False, num_devices=1)
    f32 = mybir.dt.float32
    args = [nc.dram_tensor(name, a.shape, f32, kind="ExternalInput").ap() for name, a in arrays.items()]
    out_direct = nc.dram_tensor("out_direct", (O2, tiles, BT), f32, kind="ExternalOutput").ap()
    out_second = nc.dram_tensor("out_second", (O2, tiles, BT), f32, kind="ExternalOutput").ap()
    build(nc, *args, out_direct, out_second)
    result = run(nc, [arrays], core_ids=[0]).results[0]
    direct = result["out_direct"].reshape(O2, tiles * BT)
    second = result["out_second"].reshape(O2, tiles * BT)
    return np.ascontiguousarray(np.concatenate([direct, second], axis=0).T)
```
